# Optimizing a Trainium2 kernel written in Bass

```python
import numpy as np
import jax
import jax.numpy as jnp

def _softmax(x, axis=-1):
    return jax.nn.softmax(x, axis=axis)

def _gelu(x):
    return jax.nn.gelu(x, approximate=True)

def _silu(x):
    return jax.nn.silu(x)

def _sigmoid(x):
    return jax.nn.sigmoid(x)

def _layernorm(x, axis=-1, eps=1e-05):
    m = jnp.mean(x, axis=axis, keepdims=True)
    v = jnp.var(x, axis=axis, keepdims=True)
    return (x - m) / jnp.sqrt(v + eps)

def _scatter_add(tgt, idx, src, axis=0):
    return tgt.at[idx].add(src)

def _segment_sum(src, seg, n):
    return jax.ops.segment_sum(src, seg, n)
kernel_name = 'mk_adj_preln_d1_adj_r2_80d248'

def setup_inputs(seed: int=0):
    np.random.seed(seed)
    _w = jnp.asarray

    def _rec_inputs():
        import jax
        import jax.numpy as jnp
        _gk = jax.random.key(seed)
        x = -0.0004776 + 1.001 * jax.random.normal(jax.random.fold_in(_gk, 1), (1354, 512), jnp.float32)
        _a = jax.random.bernoulli(jax.random.fold_in(_gk, 2), 0.00590842, (1354, 1354))
        _a = jnp.logical_or(_a, jnp.swapaxes(_a, -1, -2))
        _a = jnp.logical_or(_a, jnp.eye(1354, dtype=bool))
        _af = _a.astype(jnp.float32)
        adj = _af
        return (x, adj)
    x, adj = _rec_inputs()

    def _L0_gnn_setup():
        import jax, jax.numpy as jnp
        import numpy as np
        N, H, E, HEADS = (1500, 512, 10000, 8)
        DK = H // HEADS
        key = jax.random.key(seed)
        k1, k2, k3, k4 = jax.random.split(key, 4)
        inst_feature = jax.random.normal(k1, (N, H), dtype=jnp.float32)
        rel_pair_index = jax.random.randint(k2, (E, 2), 0, N, dtype=jnp.int64)
        agg = jnp.zeros((N, N), dtype=jnp.float32)
        agg = agg.at[rel_pair_index[:, 0], rel_pair_index[:, 1]].set(1.0)
        agg = agg.at[jnp.arange(N), jnp.arange(N)].set(1.0)
        std = float(np.sqrt(2.0 / (H + DK)))
        Wq = jax.random.normal(k3, (H, H), dtype=jnp.float32) * std
        Wk = jax.random.normal(k4, (H, H), dtype=jnp.float32) * std
        bq = jnp.zeros((H,), dtype=jnp.float32)
        bk = jnp.zeros((H,), dtype=jnp.float32)
        return {'inst_feature': inst_feature, 'aggregator_matrix': agg, 'rel_pair_index': rel_pair_index, 'Wq': Wq, 'bq': bq, 'Wk': Wk, 'bk': bk}
    _L0_gnn_all = _L0_gnn_setup()
    _L0_gnn_in = {k: v for k, v in _L0_gnn_all.items() if k in ('rel_pair_index', 'Wq', 'bq', 'Wk', 'bk')}
    del _L0_gnn_all
    return {'x': x, 'adj': adj, 'L0_gnn_rel_pair_index': _L0_gnn_in['rel_pair_index'], 'L0_gnn_Wq': _L0_gnn_in['Wq'], 'L0_gnn_bq': _L0_gnn_in['bq'], 'L0_gnn_Wk': _L0_gnn_in['Wk'], 'L0_gnn_bk': _L0_gnn_in['bk']}

def reference(x, adj, L0_gnn_rel_pair_index, L0_gnn_Wq, L0_gnn_bq, L0_gnn_Wk, L0_gnn_bk):
    import jax
    import jax.numpy as jnp

    def _L0_gnn_ref(inst_feature, aggregator_matrix, rel_pair_index, Wq, bq, Wk, bk):
        import jax, jax.numpy as jnp
        import numpy as np
        N, H, E, HEADS = (1500, 512, 10000, 8)
        DK = H // HEADS
        n = inst_feature.shape[0]
        sub = rel_pair_index[:, 0]
        obj = rel_pair_index[:, 1]
        q = (inst_feature[sub] @ Wq.T + bq).reshape(-1, HEADS, DK)
        k = (inst_feature[obj] @ Wk.T + bk).reshape(-1, HEADS, DK)
        att = ((q * k).sum(-1) / np.sqrt(DK)).T.astype(inst_feature.dtype)
        scores = jnp.zeros((HEADS, n, n), dtype=inst_feature.dtype)
        scores = scores.at[:, sub, obj].set(att)
        mask = (1.0 - aggregator_matrix).astype(bool)
        scores = jnp.where(mask[None], -jnp.inf, scores)
        di = jnp.arange(n)
        scores = scores.at[:, di, di].set(1e-07)
        attn = jax.nn.softmax(scores, axis=2)
        aggregator_factor = attn.sum(axis=0) / HEADS
        return aggregator_factor @ inst_feature
    h = jnp.maximum(_layernorm(x, axis=-1), 0.0)
    x = x + _L0_gnn_ref(h, adj, L0_gnn_rel_pair_index, L0_gnn_Wq, L0_gnn_bq, L0_gnn_Wk, L0_gnn_bk)
    return x

_drawn_inputs = setup_inputs


def setup_inputs(seed=0):
    import zlib

    import numpy as np

    out = dict(_drawn_inputs(seed))
    spreads = {'L0_gnn_bq': (0.0, 0.8), 'L0_gnn_bk': (0.0, 0.8)}
    factors = {'L0_gnn_Wq': 8.0, 'L0_gnn_Wk': 8.0}
    for name, (base, spread) in spreads.items():
        noise = np.random.default_rng([zlib.crc32(name.encode()), seed]).standard_normal(out[name].shape)
        drawn = base * np.exp(spread * noise) if base else spread * noise
        out[name] = jnp.asarray(drawn.astype(out[name].dtype))
    for name, factor in factors.items():
        out[name] = (out[name] * factor).astype(out[name].dtype)
    return out
```

```python
def build(nc, x, adj, pairs, Wq, bq, Wk, bk, out, h_dram, ah_dram, pair_dram):
    import numpy as np
    import concourse.bass as bass
    from concourse import mybir
    from contextlib import ExitStack

    fp32, fp16, i32 = mybir.dt.float32, mybir.dt.float16, mybir.dt.int32
    ALU, ACT, AX = mybir.AluOpType, mybir.ActivationFunctionType, mybir.AxisListType

    P = 128
    N, H = x.shape
    HEADS = 8
    DK = H // HEADS
    T = (N + P - 1) // P
    LAST = N - (T - 1) * P
    FULL = T - 1
    CC = H // P
    E = pairs.shape[0]
    EP = 125
    EC = E // EP
    SLOTS = 128
    TOP = 8
    EPS = 1e-5
    DIAG = 1e-7
    SCALE = 1.0 / DK ** 0.5
    SPLIT = 2048.0
    E0 = float(np.exp(np.float32(0.0) - np.float32(DIAG)))
    NOWHERE = 1 << 22
    BIG = 1e38
    GROUPS = [(0, 4), (4, 8), (8, T)]
    ABUF, TBUF = 3, 3

    def rows(t):
        return P if t < FULL else LAST

    def flat(ap):
        return ap.rearrange("a b -> (a b)").rearrange("(n o) -> n o", o=1)

    def norm_parts(a, b):
        return [(a, b, P)] if b < T else [(a, FULL, P), (FULL, T, LAST)]

    ctx = ExitStack()
    with ctx:
        def sb(name, shape, dt=fp32):
            return ctx.enter_context(nc.sbuf_tensor(name, shape, dt))

        def pb(name, shape, dt=fp32):
            return ctx.enter_context(nc.psum_tensor(name, shape, dt))

        def sem(name):
            return ctx.enter_context(nc.semaphore(name))

        pair_i = sb("pair_i", [EP, EC, 2], i32)
        pair_f = sb("pair_f", [EP, EC, 2])
        neg = sb("neg", [EP, EC, 2])
        inside = sb("inside", [EP, EC, 2])
        pair_at = sb("pair_at", [EP, EC])
        pair_at_i = sb("pair_at_i", [EP, EC], i32)
        counts_pair = sb("counts_pair", [EP, EC])
        pair_code = sb("pair_code", [EP, EC])
        adj_at = sb("adj_at", [EP, EC])
        hit = sb("hit", [EP, EC])
        hit_code = sb("hit_code", [EP, EC])
        top_code = sb("top_code", [EP, TOP])
        hit_count = sb("hit_count", [EP, 2])
        col_less_row = sb("col_less_row", [P, P])
        slot_less_s = sb("slot_less_s", [P, TOP, SLOTS])
        ident = sb("ident", [P, P])
        ident16 = sb("ident16", [P, P], fp16)
        off_diag16 = sb("off_diag16", [P, P], fp16)
        before = sb("before", [P, P])
        after = sb("after", [P, P])
        ones = sb("ones", [P, P])
        bias_row = sb("bias_row", [1, 2, H])
        xt = sb("xt", [P, T, H])
        ht = sb("ht", [P, T, H])
        h_hi = sb("h_hi", [P, T, H], fp16)
        h_lo = sb("h_lo", [P, T, H], fp16)
        stats = sb("stats", [P, T, 6])
        mv = sb("mv", [P, T, 2])
        var_eps = sb("var_eps", [P, T])
        std = sb("std", [P, T])
        rstd = sb("rstd", [P, T])
        nmr = sb("nmr", [P, T])
        w_raw = sb("w_raw", [P, 2, CC, H])
        w_t = sb("w_t", [P, 2, CC, H])
        a_raw = sb("a_raw", [P, ABUF, N])
        a16 = sb("a16", [P, TBUF, N], fp16)
        a_t = sb("a_t", [P, TBUF, T, P], fp16)
        count_junk = sb("count_junk", [P, N], fp16)
        ah = sb("ah", [P, T, H + 1])
        den = sb("den", [P, T])
        w_diag = sb("w_diag", [P, T])
        w_nbr = sb("w_nbr", [P, T])
        o_t = sb("o_t", [P, TBUF, H])
        at_slot = sb("at_slot", [EP, TOP, SLOTS])
        p_base = sb("p_base", [P, 1])
        over = sb("over", [P, 2])
        over_i = sb("over_i", [P, 1], i32)
        code = sb("code", [P, 1])
        filled = sb("filled", [P, 1])
        sc = sb("sc", [P, 8])
        sub_i = sb("sub_i", [P, 1], i32)
        obj_i = sb("obj_i", [P, 1], i32)
        row_i = sb("row_i", [P, 1], i32)
        spread = sb("spread", [P, 2, P])
        same_row = sb("same_row", [P, P])
        same_row_lim = sb("same_row_lim", [P, P])
        earlier_same = sb("earlier_same", [P, P])
        same_code = sb("same_code", [P, P])
        h_sub = sb("h_sub", [P, H])
        h_obj = sb("h_obj", [P, H])
        x_sub = sb("x_sub", [P, H])
        ah_sub = sb("ah_sub", [P, H + 1])
        hs_t = sb("hs_t", [P, 2, CC, P])
        q_s = w_raw[:, 0, 2:4, :].rearrange("p o c -> p (o c)")[:, 0:H]
        prod = sb("prod", [P, H])
        score = sb("score", [P, HEADS])
        s_diag = w_raw[:, 0, :, :].rearrange("p o c -> p (o c)")[:, 0:HEADS * P].rearrange("p (h e) -> p h e", h=HEADS)
        s_lim = w_raw[:, 1, :, :].rearrange("p o c -> p (o c)")[:, 0:HEADS * P].rearrange("p (h e) -> p h e", h=HEADS)
        mx = sb("mx", [P, HEADS])
        expo = sb("expo", [P, 3, HEADS])
        ex = sb("ex", [P, 3, HEADS])
        ew = sb("ew", [P, HEADS + 1])
        dn = sb("dn", [P, HEADS])
        part = sb("part", [P, 3, HEADS])
        wts = sb("wts", [P, 3])
        y = sb("y", [P, H])
        zero_w = sb("zero_w", [P, 1])
        warm = sb("warm", [P, 1])

        p_tr = [pb("p_tr0", [P, 2048], fp16), pb("p_tr1", [P, 2048], fp16)]
        p_ah = [pb("p_ah0", [P, H]), pb("p_ah1", [P, H])]
        p_w = [pb("p_w0", [P, H]), pb("p_w1", [P, H])]
        p_rows = p_tr[0][:, :].bitcast(fp32)
        p_sum = p_tr[0][:, :].bitcast(fp32)[:, 512:512 + HEADS + 1]
        p_srow = p_tr[1][:, :].bitcast(fp32)

        pairs_in = sem("pairs_in")
        x_in = [sem(f"x_in{g}") for g in range(len(GROUPS))]
        w_in = sem("w_in")
        bias_in = sem("bias_in")
        a_in = [sem(f"a_in{b}") for b in range(ABUF)]
        iotas = sem("iotas")
        consts = sem("consts")
        at_ready = sem("at_ready")
        adj_got = sem("adj_got")
        var_ready = sem("var_ready")
        std_ready = sem("std_ready")
        norm_ready = sem("norm_ready")
        h_ready = sem("h_ready")
        h_split = sem("h_split")
        h_stored = sem("h_stored")
        w_turned = sem("w_turned")
        w_kept = sem("w_kept")
        a_masked = sem("a_masked")
        a_counted = sem("a_counted")
        a_turned = sem("a_turned")
        a_t_kept = sem("a_t_kept")
        ah_done = sem("ah_done")
        ah_kept = sem("ah_kept")
        ah_stored = sem("ah_stored")
        o_ready = sem("o_ready")
        o_stored = [sem(f"o_stored{b}") for b in range(TBUF)]
        dve_step = sem("dve_step")
        hits_ready = sem("hits_ready")
        base_done = sem("base_done")
        onehot_ready = sem("onehot_ready")
        code_done = sem("code_done")
        slots_ready = sem("slots_ready")
        spread_ready = sem("spread_ready")
        rows_done = sem("rows_done")
        got_h = sem("got_h")
        got_x = sem("got_x")
        got_ah = sem("got_ah")
        hs_turned = sem("hs_turned")
        hs_kept = sem("hs_kept")
        q_done = sem("q_done")
        k_done = sem("k_done")
        q_kept = sem("q_kept")
        sdiag_ready = sem("sdiag_ready")
        srow_done = sem("srow_done")
        expo_ready = sem("expo_ready")
        ex_ready = sem("ex_ready")
        ew_ready = sem("ew_ready")
        sum_done = sem("sum_done")
        v_ready = sem("v_ready")
        y_done = sem("y_done")
        y_ready = sem("y_ready")
        rows_written = sem("rows_written")

        x_tiles = x[0:FULL * P, :].rearrange("(t p) c -> p t c", p=P)
        h_tiles = h_dram[0:FULL * P, :].rearrange("(t p) c -> p t c", p=P)

        block = nc.Block()
        block.__enter__()

        @block.sync
        def _(sp):
            sp.dma_start(pair_i[:], pairs.rearrange("(p e) c -> p e c", p=EP)).then_inc(pairs_in, 16)
            for g, (a, b) in enumerate(GROUPS):
                full = min(b, FULL)
                sp.dma_start(xt[:, a:full, :], x_tiles[:, a:full, :]).then_inc(x_in[g], 16)
                if b == T:
                    sp.dma_start(xt[0:LAST, FULL, :], x[FULL * P:N, :]).then_inc(x_in[g], 16)
                if g == 0:
                    for n, w in enumerate((Wq, Wk)):
                        sp.dma_start(w_raw[:, n, :, :], w.rearrange("(o p) c -> p o c", p=P)).then_inc(w_in, 16)
            for n, b in enumerate((bq, bk)):
                sp.dma_start(bias_row[0:1, n, :], b.rearrange("(o c) -> o c", o=1)).then_inc(bias_in, 16)

            def load_a(t):
                if t >= ABUF:
                    sp.wait_ge(a_masked, t - ABUF + 1)
                sp.dma_start(a_raw[0:rows(t), t % ABUF, :], adj[t * P:t * P + rows(t), :]).then_inc(a_in[t % ABUF], 16)

            for t in range(ABUF):
                load_a(t)
            for g, (a, b) in enumerate(GROUPS):
                sp.wait_ge(h_ready, b)
                full = min(b, FULL)
                sp.dma_start(h_tiles[:, a:full, :], ht[:, a:full, :]).then_inc(h_stored, 16)
                if b == T:
                    sp.dma_start(h_dram[FULL * P:N, :], ht[0:LAST, FULL, :]).then_inc(h_stored, 16)
            for t in range(ABUF, T + 1):
                if t < T:
                    load_a(t)
                for u in ([t - ABUF] if t < T else range(T - ABUF, T)):
                    r = rows(u)
                    sp.wait_ge(ah_kept, u + 1)
                    sp.dma_start(ah_dram[u * P:u * P + r, :], ah[0:r, u, :]).then_inc(ah_stored, 16)
                    sp.wait_ge(o_ready, u + 1)
                    sp.dma_start(out[u * P:u * P + r, :], o_t[0:r, u % TBUF, :]).then_inc(o_stored[u % TBUF], 16)

        @block.gpsimd
        def _(pool):
            nc.gpsimd.iota(col_less_row[:], [[1, P]], base=0, channel_multiplier=-1,
                           allow_small_or_imprecise_dtypes=True).then_inc(iotas, 1)
            pool.wait_ge(at_ready, 1)
            for c in range(EC):
                pool.indirect_dma_start(adj_at[:, c:c + 1], None, flat(adj),
                                        bass.IndirectOffsetOnAxis(ap=pair_at_i[:, c:c + 1], axis=0),
                                        bounds_check=N * N - 1, oob_is_err=False).then_inc(adj_got, 16)
                if c == 0:
                    nc.gpsimd.iota(slot_less_s[:], [[-1, TOP], [1, SLOTS]], base=0, channel_multiplier=0,
                                   allow_small_or_imprecise_dtypes=True).then_inc(iotas, 1)
            pool.wait_ge(h_stored, 16 * (len(GROUPS) + 1))
            pool.wait_ge(slots_ready, 1)
            for dst, at in ((h_sub, sub_i), (h_obj, obj_i)):
                pool.indirect_dma_start(dst[:], None, h_dram, bass.IndirectOffsetOnAxis(ap=at[:], axis=0),
                                        bounds_check=N - 1, oob_is_err=False).then_inc(got_h, 16)
            pool.indirect_dma_start(x_sub[:], None, x, bass.IndirectOffsetOnAxis(ap=sub_i[:], axis=0),
                                    bounds_check=N - 1, oob_is_err=False).then_inc(got_x, 16)
            pool.wait_ge(ah_stored, 16 * T)
            pool.indirect_dma_start(ah_sub[:], None, ah_dram, bass.IndirectOffsetOnAxis(ap=sub_i[:], axis=0),
                                    bounds_check=N - 1, oob_is_err=False).then_inc(got_ah, 16)
            for b in range(TBUF):
                pool.wait_ge(o_stored[b], 16 * len(range(b, T, TBUF)))
            pool.wait_ge(y_ready, 1)
            pool.indirect_dma_start(out, bass.IndirectOffsetOnAxis(ap=row_i[:], axis=0), y[:], None,
                                    bounds_check=N - 1, oob_is_err=False).then_inc(rows_written, 16)
            pool.wait_ge(rows_written, 16)

        @block.scalar
        def _(act):
            def turn_w(k0, k1):
                for k in range(k0, k1):
                    act.wait_ge(w_turned, k + 1)
                    nc.scalar.activation(w_t[:, k // CC, k % CC, :], p_w[k % 2][:], ACT.Copy).then_inc(w_kept, 1)

            for g, (a, b) in enumerate(GROUPS):
                act.wait_ge(x_in[g], 32 if b == T else 16)
                act.wait_ge(var_ready, g + 1)
                for u, v, r in norm_parts(a, b):
                    last = nc.scalar.activation(std[0:r, u:v], var_eps[0:r, u:v], ACT.Sqrt)
                last.then_inc(std_ready, 1)
                act.wait_ge(norm_ready, g + 1)
                for t in range(a, b):
                    r = rows(t)
                    nc.scalar.activation(ht[0:r, t, :], xt[0:r, t, :], ACT.Relu, bias=nmr[0:r, t:t + 1],
                                         scale=rstd[0:r, t:t + 1]).then_inc(h_ready, 1)
                if g < 2:
                    turn_w(CC * g, CC * g + CC)

            def keep_ah(t):
                r = rows(t)
                act.wait_ge(ah_done, t + 1)
                nc.scalar.activation(ah[0:r, t, 0:H], p_ah[t % 2][0:r, :], ACT.Copy,
                                     scale=1.0 / SPLIT).then_inc(ah_kept, 1)

            for t in range(T):
                r = rows(t)
                act.wait_ge(a_turned, t + 1)
                if t >= TBUF:
                    act.wait_ge(ah_done, t - TBUF + 1)
                nc.scalar.activation(a_t[:, t % TBUF, 0:FULL, 0:r],
                                     p_tr[t % 2][:, 0:FULL * P].rearrange("p (j i) -> p j i", i=P)[:, :, 0:r], ACT.Copy)
                nc.scalar.activation(a_t[0:LAST, t % TBUF, FULL, 0:r],
                                     p_tr[t % 2][0:LAST, FULL * P:FULL * P + r], ACT.Copy).then_inc(a_t_kept, 1)
                if t >= 1:
                    act.wait_ge(a_counted, t)
                nc.scalar.activation(count_junk[0:r, :], a16[0:r, t % TBUF, :], ACT.Copy,
                                     accum_out=ah[0:r, t, H:H + 1]).then_inc(a_counted, 1)
                if t >= 1:
                    keep_ah(t - 1)
            keep_ah(T - 1)

            act.wait_ge(consts, 1)
            nc.scalar.activation(warm[:], zero_w[:], ACT.Exp)
            for n in range(2):
                act.wait_ge(hs_turned, n + 1)
                nc.scalar.activation(hs_t[:, n, :, :], p_w[n][:].rearrange("p (c s) -> p c s", c=CC),
                                     ACT.Copy).then_inc(hs_kept, 1)
            act.wait_ge(q_done, 1)
            nc.scalar.activation(q_s, p_ah[0][:], ACT.Copy).then_inc(q_kept, 1)
            act.wait_ge(expo_ready, 1)
            nc.scalar.activation(ex[:], expo[:], ACT.Exp).then_inc(ex_ready, 1)

        @block.tensor
        def _(pe):
            pe.wait_ge(consts, 1)
            pe.wait_ge(w_in, 32)
            for k in range(2 * CC):
                if k >= 2:
                    pe.wait_ge(w_kept, k - 1)
                for o in range(CC):
                    last = nc.tensor.transpose(p_w[k % 2][:, o * P:(o + 1) * P],
                                               w_raw[:, k // CC, o, (k % CC) * P:(k % CC + 1) * P], ident[:])
                last.then_inc(w_turned, 1)

            def turn_a(t):
                r = rows(t)
                pe.wait_ge(a_masked, t + 1)
                if t >= 2:
                    pe.wait_ge(a_t_kept, t - 1)
                for j in range(T):
                    last = nc.tensor.transpose(p_tr[t % 2][0:rows(j), j * P:j * P + r],
                                               a16[0:r, t % TBUF, j * P:j * P + rows(j)], ident16[0:r, 0:r])
                last.then_inc(a_turned, 1)

            turn_a(0)
            for t in range(T):
                if t + 1 < T:
                    turn_a(t + 1)
                r = rows(t)
                pe.wait_ge(a_t_kept, t + 1)
                if t >= 2:
                    pe.wait_ge(ah_kept, t - 1)
                for j in range(T):
                    if t == 0:
                        pe.wait_ge(h_split, j + 1)
                    for half in (h_hi, h_lo):
                        last = nc.tensor.matmul(p_ah[t % 2][0:r, :], a_t[0:rows(j), t % TBUF, j, 0:r],
                                                half[0:rows(j), j, :], start=(j == 0 and half is h_hi),
                                                stop=(j == T - 1 and half is h_lo))
                last.then_inc(ah_done, 1)

            pe.wait_ge(hits_ready, 1)
            nc.tensor.matmul(p_w[0][:, 0:1], before[0:EP, :], hit_count[:, 0:1], start=True, stop=True)
            nc.tensor.matmul(p_w[0][:, 1:3], ones[0:EP, :], hit_count[:, 0:2], start=True, stop=True,
                             skip_group_check=True).then_inc(base_done, 1)
            pe.wait_ge(onehot_ready, 1)
            for s in range(TOP):
                last = nc.tensor.matmul(p_w[1][:, 0:1], at_slot[:, s, :], top_code[:, s:s + 1],
                                        start=(s == 0), stop=(s == TOP - 1))
            last.then_inc(code_done, 1)
            pe.wait_ge(spread_ready, 1)
            pe.wait_ge(a_t_kept, T)
            nc.tensor.matmul(p_rows[:, 0:2 * P], ones[:], spread[:].rearrange("p a b -> p (a b)"),
                             start=True, stop=True).then_inc(rows_done, 1)
            pe.wait_ge(bias_in, 32)
            pe.wait_ge(ah_kept, T)
            for n in range(2):
                nc.tensor.matmul(p_ah[n][:], ones[0:1, :], bias_row[0:1, n, :], start=True, stop=False)
            for n, src in enumerate((h_sub, h_obj)):
                pe.wait_ge(got_h, 32)
                for c in range(CC):
                    last = nc.tensor.transpose(p_w[n][:, c * P:(c + 1) * P], src[:, c * P:(c + 1) * P], ident[:])
                last.then_inc(hs_turned, 1)
            for n, done in enumerate((q_done, k_done)):
                pe.wait_ge(hs_kept, n + 1)
                for c in range(CC):
                    last = nc.tensor.matmul(p_ah[n][:], hs_t[:, n, c, :], w_t[:, n, c, :], start=False,
                                            stop=(c == CC - 1))
                last.then_inc(done, 1)
            pe.wait_ge(sdiag_ready, 1)
            for n in range(2):
                last = nc.tensor.matmul(p_srow[:, n * 512:(n + 1) * 512], ones[:],
                                        s_diag[:, 4 * n:4 * n + 4, :].rearrange("p h e -> p (h e)"),
                                        start=True, stop=True)
            last.then_inc(srow_done, 1)
            pe.wait_ge(ew_ready, 1)
            nc.tensor.matmul(p_sum, same_row[:], ew[:], start=True, stop=True).then_inc(sum_done, 1)
            pe.wait_ge(v_ready, 1)
            nc.tensor.matmul(p_w[0][:], same_row[:], prod[:], start=True, stop=True).then_inc(y_done, 1)

        @block.vector
        def _(dve):
            V = nc.vector
            steps = [0]

            def then_wait(ins):
                steps[0] += 1
                ins.then_inc(dve_step, 1)
                dve.wait_ge(dve_step, steps[0])

            dve.wait_ge(pairs_in, 16)
            then_wait(V.tensor_copy(pair_f[:], pair_i[:]))
            then_wait(V.tensor_scalar(neg[:], pair_f[:], 0.0, float(N), ALU.is_lt, ALU.mult))
            then_wait(V.tensor_tensor(pair_f[:], pair_f[:], neg[:], ALU.add))
            V.tensor_scalar(inside[:], pair_f[:], float(N - 1), None, ALU.is_le)
            then_wait(V.tensor_scalar(neg[:], pair_f[:], 0.0, float(N - 1), ALU.max, ALU.min))
            then_wait(V.scalar_tensor_tensor(out=pair_at[:], in0=neg[:, :, 0], scalar=float(N), in1=neg[:, :, 1],
                                             op0=ALU.mult, op1=ALU.add))
            V.tensor_copy(pair_at_i[:], pair_at[:]).then_inc(at_ready, 1)
            then_wait(V.scalar_tensor_tensor(out=inside[:], in0=pair_f[:], scalar=0.0, in1=inside[:],
                                             op0=ALU.is_ge, op1=ALU.mult))
            then_wait(V.tensor_tensor(counts_pair[:], inside[:, :, 0], inside[:, :, 1], ALU.mult))
            then_wait(V.tensor_tensor(pair_code[:], pair_f[:, :, 0], pair_f[:, :, 1], ALU.not_equal))
            then_wait(V.tensor_tensor(counts_pair[:], counts_pair[:], pair_code[:], ALU.mult))
            V.scalar_tensor_tensor(out=pair_code[:], in0=pair_at[:], scalar=1.0, in1=counts_pair[:],
                                   op0=ALU.add, op1=ALU.mult)
            V.memset(ones[:], 1.0)
            dve.wait_ge(iotas, 1)
            V.tensor_scalar(ident16[:], col_less_row[:], 0.0, None, ALU.is_equal)
            V.tensor_scalar(off_diag16[:], col_less_row[:], 0.0, None, ALU.not_equal)
            V.tensor_scalar(before[:], col_less_row[:], 0.0, None, ALU.is_gt)
            V.tensor_scalar(after[:], col_less_row[:], 0.0, None, ALU.is_lt)
            then_wait(V.tensor_scalar(ident[:], col_less_row[:], 0.0, None, ALU.is_equal))
            V.memset(zero_w[:], 0.0).then_inc(consts, 1)

            def norm(g):
                a, b = GROUPS[g]
                dve.wait_ge(x_in[g], 32 if b == T else 16)
                for t in range(a, b):
                    r = rows(t)
                    last = V.bn_stats(stats[0:r, t, :], xt[0:r, t, :])
                then_wait(last)
                for t in range(a, b):
                    r = rows(t)
                    last = V.bn_aggr(mv[0:r, t, :], stats[0:r, t, :])
                then_wait(last)
                parts = norm_parts(a, b)
                for u, v, r in parts:
                    last = V.tensor_scalar(var_eps[0:r, u:v], mv[0:r, u:v, 1], EPS, None, ALU.add)
                last.then_inc(var_ready, 1)
                dve.wait_ge(std_ready, g + 1)
                for u, v, r in parts:
                    last = V.reciprocal(rstd[0:r, u:v], std[0:r, u:v])
                then_wait(last)
                for u, v, r in parts:
                    last = V.scalar_tensor_tensor(out=nmr[0:r, u:v], in0=mv[0:r, u:v, 0], scalar=-1.0,
                                                  in1=rstd[0:r, u:v], op0=ALU.mult, op1=ALU.mult)
                last.then_inc(norm_ready, 1)

            def split(g):
                for t in range(*GROUPS[g]):
                    r = rows(t)
                    dve.wait_ge(h_ready, t + 1)
                    then_wait(V.tensor_scalar(h_hi[0:r, t, :], ht[0:r, t, :], SPLIT, None, ALU.mult))
                    V.scalar_tensor_tensor(out=h_lo[0:r, t, :], in0=ht[0:r, t, :], scalar=SPLIT,
                                           in1=h_hi[0:r, t, :], op0=ALU.mult, op1=ALU.subtract).then_inc(h_split, 1)

            def mask(t):
                r = rows(t)
                dve.wait_ge(a_in[t % ABUF], 16 * (t // ABUF + 1))
                if t >= TBUF:
                    dve.wait_ge(a_turned, t - TBUF + 1)
                    dve.wait_ge(a_counted, t - TBUF + 1)
                then_wait(V.tensor_scalar(a16[0:r, t % TBUF, :], a_raw[0:r, t % ABUF, :], 1.0, None, ALU.is_equal))
                own = a16[0:r, t % TBUF, t * P:t * P + r]
                V.tensor_tensor(own, own, off_diag16[0:r, 0:r], ALU.mult).then_inc(a_masked, 1)

            def plain_rows(t):
                r = rows(t)
                dve.wait_ge(a_counted, t + 1)
                then_wait(V.tensor_scalar(den[0:r, t:t + 1], ah[0:r, t, H:H + 1], E0, 1.0, ALU.mult, ALU.add))
                then_wait(V.reciprocal(w_diag[0:r, t:t + 1], den[0:r, t:t + 1]))
                V.tensor_scalar(w_nbr[0:r, t:t + 1], w_diag[0:r, t:t + 1], E0, None, ALU.mult)
                if t >= TBUF:
                    dve.wait_ge(o_stored[t % TBUF], 16 * (t // TBUF))
                then_wait(V.scalar_tensor_tensor(out=o_t[0:r, t % TBUF, :], in0=ht[0:r, t, :],
                                                 scalar=w_diag[0:r, t:t + 1], in1=xt[0:r, t, :],
                                                 op0=ALU.mult, op1=ALU.add))
                dve.wait_ge(ah_kept, t + 1)
                V.scalar_tensor_tensor(out=o_t[0:r, t % TBUF, :], in0=ah[0:r, t, 0:H],
                                       scalar=w_nbr[0:r, t:t + 1], in1=o_t[0:r, t % TBUF, :],
                                       op0=ALU.mult, op1=ALU.add).then_inc(o_ready, 1)

            norm(0)
            norm(1)
            split(0)
            norm(2)
            split(1)
            mask(0)
            split(2)
            mask(1)
            for t in range(T):
                if t + 2 < T:
                    mask(t + 2)
                plain_rows(t)

            dve.wait_ge(adj_got, 16 * EC)
            V.scalar_tensor_tensor(out=hit[:], in0=adj_at[:], scalar=1.0, in1=counts_pair[:], op0=ALU.is_equal,
                                   op1=ALU.mult, accum_out=hit_count[:, 0:1])
            then_wait(V.scalar_tensor_tensor(out=hit_code[:], in0=adj_at[:], scalar=1.0, in1=pair_code[:],
                                             op0=ALU.is_equal, op1=ALU.mult))
            V.max(top_code[:], hit_code[:])
            V.tensor_scalar(hit_count[:, 1:2], hit_count[:, 0:1], TOP + 0.5, None, ALU.is_gt).then_inc(hits_ready, 1)
            dve.wait_ge(base_done, 1)
            then_wait(V.tensor_copy(p_base[:], p_w[0][:, 0:1]))
            dve.wait_ge(iotas, 2)
            V.tensor_scalar(at_slot[:], slot_less_s[0:EP, :, :], p_base[0:EP, :], None,
                            ALU.is_equal).then_inc(onehot_ready, 1)
            then_wait(V.tensor_scalar(over[:, 0:1], p_w[0][:, 1:2], SLOTS + 0.5, None, ALU.is_gt))
            then_wait(V.tensor_tensor(over[:, 1:2], p_w[0][:, 2:3], over[:, 0:1], ALU.add))
            V.tensor_scalar(over_i[:], over[:, 1:2], 0.5, None, ALU.is_gt)
            dve.wait_ge(code_done, 1)
            then_wait(V.tensor_copy(code[:], p_w[1][:, 0:1]))
            V.tensor_scalar(filled[:], code[:], 0.5, None, ALU.is_gt)
            at, quot, sub, obj, own_row, own_at = (sc[:, i:i + 1] for i in range(6))
            then_wait(V.tensor_scalar(at, code[:], -1.0, 0.0, ALU.add, ALU.max))
            then_wait(V.tensor_scalar(quot, at, 0.5, 1.0 / N, ALU.add, ALU.mult))
            then_wait(V.tensor_scalar(quot, quot, -0.5, 8388608.0, ALU.add, ALU.add))
            then_wait(V.tensor_scalar(sub, quot, -8388608.0, None, ALU.add))
            then_wait(V.scalar_tensor_tensor(out=obj, in0=sub, scalar=float(-N), in1=at, op0=ALU.mult, op1=ALU.add))
            V.tensor_copy(sub_i[:], sub)
            V.tensor_copy(obj_i[:], obj).then_inc(slots_ready, 1)
            V.scalar_tensor_tensor(out=own_row, in0=sub, scalar=1.0, in1=filled[:], op0=ALU.add, op1=ALU.mult)
            then_wait(V.tensor_copy(own_at, code[:]))
            V.tensor_scalar(spread[:, 0, :], ident[:], own_row, None, ALU.mult)
            V.tensor_scalar(spread[:, 1, :], ident[:], own_at, None, ALU.mult).then_inc(spread_ready, 1)
            dve.wait_ge(rows_done, 1)
            V.tensor_scalar(same_row[:], p_rows[:, 0:P], own_row, None, ALU.is_equal)
            then_wait(V.tensor_scalar(same_code[:], p_rows[:, P:2 * P], own_at, None, ALU.is_equal))
            V.tensor_tensor(earlier_same[:], same_row[:], after[:], ALU.mult)
            V.tensor_scalar(same_row_lim[:], same_row[:], 2.0 * BIG, -BIG, ALU.mult, ALU.add)
            then_wait(V.tensor_tensor(same_code[:], same_code[:], after[:], ALU.mult))
            dup, later, once, first = (sc[:, 6:7], sc[:, 7:8], p_base[:], filled[:])
            V.reduce_max(dup, same_code[:], AX.X)
            then_wait(V.reduce_max(later, earlier_same[:], AX.X))
            then_wait(V.scalar_tensor_tensor(out=once, in0=dup, scalar=0.5, in1=filled[:], op0=ALU.is_lt, op1=ALU.mult))
            then_wait(V.scalar_tensor_tensor(out=first, in0=later, scalar=0.5, in1=filled[:], op0=ALU.is_lt, op1=ALU.mult))
            then_wait(V.scalar_tensor_tensor(out=own_row, in0=sub, scalar=float(-NOWHERE), in1=first,
                                             op0=ALU.add, op1=ALU.mult))
            V.tensor_scalar(row_i[:], own_row, float(NOWHERE), None, ALU.add)

            dve.wait_ge(q_kept, 1)
            dve.wait_ge(k_done, 1)
            then_wait(V.tensor_tensor(prod[:], q_s, p_ah[1][:], ALU.mult))
            then_wait(V.reduce_sum(score[:], prod[:].rearrange("p (h d) -> p h d", h=HEADS), AX.X))
            then_wait(V.tensor_scalar(score[:], score[:], SCALE, None, ALU.mult))
            V.tensor_tensor(s_diag, ident[:].rearrange("p (o e) -> p o e", o=1).broadcast_to([P, HEADS, P]),
                            score[:].rearrange("p (h o) -> p h o", o=1).broadcast_to([P, HEADS, P]),
                            ALU.mult).then_inc(sdiag_ready, 1)
            dve.wait_ge(srow_done, 1)
            then_wait(V.tensor_tensor(s_lim, p_srow[:].rearrange("p (h e) -> p h e", h=HEADS),
                                      same_row_lim[:].rearrange("p (o e) -> p o e", o=1).broadcast_to([P, HEADS, P]),
                                      ALU.min))
            then_wait(V.reduce_max(mx[:], s_lim, AX.X))
            then_wait(V.tensor_scalar(mx[:], mx[:], DIAG, None, ALU.max))
            V.tensor_tensor(expo[:, 0, :], score[:], mx[:], ALU.subtract)
            V.tensor_scalar(expo[:, 1, :], mx[:], -1.0, None, ALU.mult)
            V.tensor_scalar(expo[:, 2, :], mx[:], -1.0, DIAG, ALU.mult, ALU.add).then_inc(expo_ready, 1)
            dve.wait_ge(ex_ready, 1)
            V.tensor_scalar(ew[:, 0:HEADS], ex[:, 0, :], once, None, ALU.mult)
            V.tensor_copy(ew[:, HEADS:HEADS + 1], once).then_inc(ew_ready, 1)
            dve.wait_ge(sum_done, 1)
            dve.wait_ge(got_ah, 16)
            then_wait(V.tensor_tensor(later, ah_sub[:, H:H + 1], p_sum[:, HEADS:HEADS + 1], ALU.subtract))
            then_wait(V.scalar_tensor_tensor(out=dn[:], in0=ex[:, 1, :], scalar=later, in1=ex[:, 2, :],
                                             op0=ALU.mult, op1=ALU.add))
            then_wait(V.tensor_tensor(dn[:], dn[:], p_sum[:, 0:HEADS], ALU.add))
            then_wait(V.reciprocal(dn[:], dn[:]))
            then_wait(V.tensor_tensor(part[:], ex[:],
                                      dn[:].rearrange("p (o h) -> p o h", o=1).broadcast_to([P, 3, HEADS]), ALU.mult))
            then_wait(V.reduce_sum(wts[:], part[:], AX.X))
            then_wait(V.tensor_scalar(wts[:], wts[:], 1.0 / HEADS, None, ALU.mult))
            then_wait(V.tensor_tensor(dup, wts[:, 0:1], wts[:, 1:2], ALU.subtract))
            then_wait(V.tensor_tensor(dup, dup, once, ALU.mult))
            V.tensor_scalar(prod[:], h_obj[:], dup, None, ALU.mult).then_inc(v_ready, 1)
            dve.wait_ge(got_x, 16)
            then_wait(V.scalar_tensor_tensor(out=y[:], in0=ah_sub[:, 0:H], scalar=wts[:, 1:2], in1=x_sub[:],
                                             op0=ALU.mult, op1=ALU.add))
            then_wait(V.scalar_tensor_tensor(out=y[:], in0=h_sub[:], scalar=wts[:, 2:3], in1=y[:],
                                             op0=ALU.mult, op1=ALU.add))
            dve.wait_ge(y_done, 1)
            V.tensor_tensor(y[:], p_w[0][:], y[:], ALU.add).then_inc(y_ready, 1)


        block.__exit__(None, None, None)
        dense_block = ctx.enter_context(nc.Block())

        d_zero = sem("d_zero")
        d_cleared = sem("d_cleared")
        d_col = sem("d_col")
        d_col_seen = sem("d_col_seen")
        d_scattered = sem("d_scattered")
        d_bias = sem("d_bias")
        k_in = sem("k_in")
        k_turned = sem("k_turned")
        k_h_kept = sem("k_h_kept")
        kt_done = sem("kt_done")
        kt_kept = sem("kt_kept")
        d_in = sem("d_in")
        d_turned = sem("d_turned")
        d_h_kept = sem("d_h_kept")
        d_q_done = sem("d_q_done")
        d_q_kept = sem("d_q_kept")
        d_s_done = sem("d_s_done")
        d_s_read = sem("d_s_read")
        d_max = sem("d_max")
        d_exp = sem("d_exp")
        d_acc_ready = sem("d_acc_ready")
        d_acc_turned = sem("d_acc_turned")
        d_acc_kept = sem("d_acc_kept")
        d_o_done = sem("d_o_done")
        d_y_ready = sem("d_y_ready")
        d_stored = sem("d_stored")
        d_iota = sem("d_iota")
        d_step = sem("d_step")
        d_next = sem("d_next")

        k_t = ah[:].rearrange("p t c -> p (t c)")[:, 0:CC * N].rearrange("p (o n) -> p o n", o=CC)
        planes = xt[:].rearrange("p t c -> p (t c)")[:, 0:4 * N].rearrange("p (k n) -> p k n", k=4)
        upper, lower, z, acc = (planes[:, k, :] for k in range(4))
        adj_rows, work, col_less_p = (a_raw[:, k, :] for k in range(3))
        pair_rows, zeros = a16[:, 0, :], a16[:, 1, :]
        h_rows, x_rows, h_rows_t, q_t = h_sub, x_sub, hs_t[:, 0, :, :], hs_t[:, 1, :, :]
        acc_t = a_t[:].rearrange("p b j i -> p (b j i)").bitcast(fp32)[:, 0:T * P].rearrange("p (j i) -> p j i", i=P)
        SA = 1024
        p_sa, p_sb = p_tr[0][:, :].bitcast(fp32), p_ah[0][:]
        hit_at_i = sb("hit_at_i", [EP, EC], i32)
        one_at = sb("one_at", [EP, 1], i32)
        one16 = sb("one16", [EP, 1], fp16)
        bias_col = sb("bias_col", [P, 2, CC])
        first_row = sb("first_row", [P, 1])
        row_max = sb("row_max", [P, 1])
        neg_max = sb("neg_max", [P, 1])
        row_sum = sb("row_sum", [P, 1])
        row_w = sb("row_w", [P, 1])
        pair_grid = pair_dram.rearrange("(n m) o -> n (m o)", m=N)

        def over_row_tiles(engine, body):
            with engine.Fori(0, FULL) as t:
                body(t, t * P)
            body(FULL, N - P)

        def needed(engine):
            return engine.If(engine.value_load(over_i[0:1, 0:1], min_val=0, max_val=1) > 0)

        @dense_block.sync
        def _(sp):
            with needed(sp):
                sp.wait_ge(d_zero, 1)
                with sp.Fori(0, FULL) as t:
                    sp.dma_start(pair_grid[bass.ts(t, P), :], zeros).then_inc(d_cleared, 16)
                sp.dma_start(pair_grid[FULL * P:N, :], zeros[0:LAST, :]).then_inc(d_cleared, 16)
                with nc.allow_non_contiguous_dma("4 values per partition"):
                    for n, b in enumerate((bq, bk)):
                        sp.dma_start(bias_col[:, n, :], b.rearrange("(o p) -> p o", p=P)).then_inc(d_bias, 16)

                def keys(t, r0):
                    sp.dma_start(h_rows[:], h_dram[bass.ds(r0, P), :]).then_inc(k_in, 16)
                    sp.wait_ge(k_turned, t + 1)
                    sp.sem_inc(d_next, 1)

                def tile(t, r0):
                    sp.dma_start(adj_rows, adj[bass.ds(r0, P), :]).then_inc(d_in, 16)
                    sp.dma_start(pair_rows, pair_grid[bass.ds(r0, P), :]).then_inc(d_in, 16)
                    sp.dma_start(h_rows[:], h_dram[bass.ds(r0, P), :]).then_inc(d_in, 16)
                    sp.dma_start(x_rows[:], x[bass.ds(r0, P), :]).then_inc(d_in, 16)
                    sp.wait_ge(d_y_ready, t + 1)
                    sp.dma_start(out[bass.ds(r0, P), :], y[:]).then_inc(d_stored, 16)
                    sp.wait_ge(d_stored, t * 16 + 16)
                    sp.sem_inc(d_next, 1)

                over_row_tiles(sp, keys)
                sp.wait_ge(d_scattered, 16 * EC)
                over_row_tiles(sp, tile)

        @dense_block.gpsimd
        def _(pool):
            with needed(pool):
                nc.gpsimd.iota(col_less_p, [[1, N]], base=0, channel_multiplier=-1,
                               allow_small_or_imprecise_dtypes=True).then_inc(d_iota, 1)
                pool.wait_ge(d_cleared, 16 * T)
                with pool.Fori(0, EC) as c:
                    pool.wait_ge(d_col, c + 1)
                    pool.sem_inc(d_col_seen, 1)
                    pool.indirect_dma_start(pair_dram, bass.IndirectOffsetOnAxis(ap=one_at[:], axis=0), one16[:], None,
                                            bounds_check=N * N - 1, oob_is_err=False).then_inc(d_scattered, 16)
                    pool.wait_ge(d_scattered, c * 16 + 16)

        @dense_block.scalar
        def _(act):
            with needed(act):
                act.wait_ge(d_bias, 32)

                def keys(t, r0):
                    act.wait_ge(k_turned, t + 1)
                    nc.scalar.activation(h_rows_t, p_w[0][:].rearrange("p (c s) -> p c s", c=CC),
                                         ACT.Copy).then_inc(k_h_kept, 1)
                    act.wait_ge(kt_done, t + 1)
                    for o in range(CC):
                        ins = nc.scalar.activation(k_t[:, o, bass.ds(r0, P)], p_w[1][:, o * P:(o + 1) * P],
                                                   ACT.Identity, bias=bias_col[:, 1, o:o + 1])
                    ins.then_inc(kt_kept, 1)

                def tile(t, r0):
                    act.wait_ge(d_turned, t + 1)
                    nc.scalar.activation(h_rows_t, p_w[0][:].rearrange("p (c s) -> p c s", c=CC),
                                         ACT.Copy).then_inc(d_h_kept, 1)
                    act.wait_ge(d_q_done, t + 1)
                    for o in range(CC):
                        ins = nc.scalar.activation(q_t[:, o, :], p_w[1][:, o * P:(o + 1) * P], ACT.Identity,
                                                   bias=bias_col[:, 0, o:o + 1])
                    ins.then_inc(d_q_kept, 1)
                    for n in range(HEADS):
                        act.wait_ge(d_max, t * HEADS + n + 1)
                        nc.scalar.activation(z, z, ACT.Exp, bias=neg_max[:], accum_out=row_sum[:]).then_inc(d_exp, 1)
                    act.wait_ge(d_acc_turned, t + 1)
                    nc.scalar.activation(acc_t[:, 0:8, :], p_tr[1][:, :].bitcast(fp32).rearrange("p (j i) -> p j i", i=P),
                                         ACT.Copy)
                    nc.scalar.activation(acc_t[:, 8:T, :], p_w[0][:, 0:(T - 8) * P].rearrange("p (j i) -> p j i", i=P),
                                         ACT.Copy).then_inc(d_acc_kept, 1)

                over_row_tiles(act, keys)
                act.wait_ge(kt_kept, T)
                over_row_tiles(act, tile)

        @dense_block.tensor
        def _(pe):
            with needed(pe):
                def turn():
                    for c in range(CC):
                        ins = nc.tensor.transpose(p_w[0][:, c * P:(c + 1) * P], h_rows[:, c * P:(c + 1) * P], ident[:])
                    return ins

                def project(n):
                    for o in range(CC):
                        for c in range(CC):
                            ins = nc.tensor.matmul(p_w[1][:, o * P:(o + 1) * P], w_t[:, n, c, o * P:(o + 1) * P],
                                                   h_rows_t[:, c, :], start=(c == 0), stop=(c == CC - 1))
                    return ins

                def keys(t, r0):
                    pe.wait_ge(k_in, t * 16 + 16)
                    turn().then_inc(k_turned, 1)
                    pe.wait_ge(k_h_kept, t + 1)
                    project(1).then_inc(kt_done, 1)
                    pe.wait_ge(kt_kept, t + 1)

                def tile(t, r0):
                    pe.wait_ge(d_in, t * 64 + 64)
                    turn().then_inc(d_turned, 1)
                    pe.wait_ge(d_h_kept, t + 1)
                    project(0).then_inc(d_q_done, 1)
                    pe.wait_ge(d_q_kept, t + 1)
                    for n in range(HEADS):
                        lo = DK * (n % 2)
                        if n:
                            pe.wait_ge(d_s_read, t * HEADS + n)
                        for a, b, dst in ((0, 512, p_sa[:, 0:512]), (512, SA, p_sa[:, 512:SA]), (SA, N, p_sb[:, 0:N - SA])):
                            ins = nc.tensor.matmul(dst, q_t[lo:lo + DK, n // 2, :], k_t[lo:lo + DK, n // 2, a:b],
                                                   start=True, stop=True)
                        ins.then_inc(d_s_done, 1)
                    pe.wait_ge(d_acc_ready, t + 1)
                    for j in range(T):
                        m = rows(j)
                        dst = p_tr[1][:, :].bitcast(fp32)[0:m, j * P:(j + 1) * P] if j < 8 else \
                            p_w[0][0:m, (j - 8) * P:(j - 7) * P]
                        ins = nc.tensor.transpose(dst, acc[:, j * P:j * P + m], ident[:])
                    ins.then_inc(d_acc_turned, 1)
                    pe.wait_ge(d_acc_kept, t + 1)
                    for j in range(T):
                        ins = nc.tensor.matmul(p_ah[1][:], acc_t[0:rows(j), j, :], ht[0:rows(j), j, :],
                                               start=(j == 0), stop=(j == T - 1))
                    ins.then_inc(d_o_done, 1)

                over_row_tiles(pe, keys)
                over_row_tiles(pe, tile)

        @dense_block.vector
        def _(dve):
            V = nc.vector
            STEPS = 8 + 5 * HEADS

            with needed(dve):
                def chain(base):
                    count = [0]

                    def then_wait(ins):
                        count[0] += 1
                        ins.then_inc(d_step, 1)
                        dve.wait_ge(d_step, base + count[0])

                    return then_wait, count

                then_wait, count = chain(0)
                V.memset(zeros, 0.0).then_inc(d_zero, 1)
                V.memset(one16[:], 1.0)
                then_wait(V.scalar_tensor_tensor(out=hit_code[:], in0=pair_at[:], scalar=float(-NOWHERE), in1=hit[:],
                                                 op0=ALU.add, op1=ALU.mult))
                then_wait(V.tensor_scalar(hit_at_i[:], hit_code[:], float(NOWHERE), None, ALU.add))
                with dve.Fori(0, EC) as c:
                    V.tensor_copy(one_at[:], hit_at_i[:, bass.ds(c, 1)]).then_inc(d_col, 1)
                    dve.wait_ge(d_scattered, c * 16 + 16)
                then_wait(V.memset(first_row[:], float(-P)))
                dve.wait_ge(d_iota, 1)
                start = count[0]

                def tile(t, r0):
                    then_wait, count = chain(t * STEPS + start)
                    dve.wait_ge(d_in, t * 64 + 64)
                    if isinstance(t, int):
                        then_wait(V.memset(first_row[:], float(N - P)))
                    else:
                        then_wait(V.tensor_scalar(first_row[:], first_row[:], float(P), None, ALU.add))
                    own = work
                    then_wait(V.tensor_scalar(adj_rows, adj_rows, 1.0, None, ALU.is_equal))
                    then_wait(V.tensor_scalar(own, col_less_p, first_row[:], None, ALU.is_equal))
                    then_wait(V.tensor_tensor(adj_rows, adj_rows, own, ALU.max))
                    then_wait(V.tensor_tensor(lower, adj_rows, pair_rows, ALU.subtract))
                    then_wait(V.tensor_scalar(lower, lower, -1.0, BIG, ALU.add, ALU.mult))
                    then_wait(V.scalar_tensor_tensor(out=lower, in0=own, scalar=DIAG, in1=lower,
                                                     op0=ALU.mult, op1=ALU.add))
                    then_wait(V.scalar_tensor_tensor(out=upper, in0=pair_rows, scalar=2.0 * BIG, in1=lower,
                                                     op0=ALU.mult, op1=ALU.add))
                    for n in range(HEADS):
                        dve.wait_ge(d_s_done, t * HEADS + n + 1)
                        V.scalar_tensor_tensor(out=z[:, 0:SA], in0=p_sa[:, 0:SA], scalar=SCALE, in1=upper[:, 0:SA],
                                               op0=ALU.mult, op1=ALU.min)
                        V.scalar_tensor_tensor(out=z[:, SA:N], in0=p_sb[:, 0:N - SA], scalar=SCALE,
                                               in1=upper[:, SA:N], op0=ALU.mult, op1=ALU.min).then_inc(d_s_read, 1)
                        dve.wait_ge(d_s_read, t * HEADS + n + 1)
                        then_wait(V.tensor_tensor(z, z, lower, ALU.max))
                        then_wait(V.reduce_max(row_max[:], z, AX.X))
                        V.tensor_scalar(neg_max[:], row_max[:], -1.0, None, ALU.mult).then_inc(d_max, 1)
                        dve.wait_ge(d_exp, t * HEADS + n + 1)
                        then_wait(V.reciprocal(row_w[:], row_sum[:]))
                        then_wait(V.tensor_scalar(row_w[:], row_w[:], 1.0 / HEADS, None, ALU.mult))
                        if n == 0:
                            then_wait(V.tensor_scalar(acc, z, row_w[:], None, ALU.mult))
                        else:
                            then_wait(V.scalar_tensor_tensor(out=acc, in0=z, scalar=row_w[:], in1=acc,
                                                             op0=ALU.mult, op1=ALU.add))
                    dve.sem_inc(d_acc_ready, 1)
                    assert count[0] == STEPS
                    dve.wait_ge(d_o_done, t + 1)
                    V.tensor_tensor(y[:], p_ah[1][:], x_rows[:], ALU.add).then_inc(d_y_ready, 1)

                over_row_tiles(dve, tile)


_INS = ['x', 'adj', 'L0_gnn_rel_pair_index', 'L0_gnn_Wq', 'L0_gnn_bq', 'L0_gnn_Wk', 'L0_gnn_bk']
_OUT_NAMES = ['out_0_dram']


def kernel(**inputs):
    import numpy as _np
    import concourse.bacc as _bacc
    from concourse import mybir as _mybir
    from concourse.bass_utils import run_bass_kernel_spmd as _run

    nc = _bacc.Bacc("TRN2", target_bir_lowering=False, num_devices=1)
    arrays, args = {}, []
    for name in _INS:
        a = _np.ascontiguousarray(inputs[name])
        arrays[f"in_{name}_dram"] = a
        args.append(nc.dram_tensor(f"in_{name}_dram", a.shape, _mybir.dt.from_np(a.dtype), kind="ExternalInput").ap())
    n, h = inputs['x'].shape
    f32, f16 = _mybir.dt.float32, _mybir.dt.float16
    args.append(nc.dram_tensor("out_0_dram", (n, h), f32, kind="ExternalOutput").ap())
    args.append(nc.dram_tensor("h_dram", (n, h), f32).ap())
    args.append(nc.dram_tensor("ah_dram", (n, h + 1), f32).ap())
    args.append(nc.dram_tensor("pair_dram", (n * n, 1), f16).ap())
    build(nc, *args)
    r = _run(nc, [arrays], core_ids=[0])
    return r.results[0]["out_0_dram"]
```
